# Optimizing a Trainium2 kernel written in Bass

```python
import numpy as np
import jax
import jax.numpy as jnp

def _softmax(x, axis=-1):
    return jax.nn.softmax(x, axis=axis)

def _gelu(x):
    return jax.nn.gelu(x, approximate=True)

def _silu(x):
    return jax.nn.silu(x)

def _sigmoid(x):
    return jax.nn.sigmoid(x)

def _layernorm(x, axis=-1, eps=1e-05):
    m = jnp.mean(x, axis=axis, keepdims=True)
    v = jnp.var(x, axis=axis, keepdims=True)
    return (x - m) / jnp.sqrt(v + eps)

def _scatter_add(tgt, idx, src, axis=0):
    return tgt.at[idx].add(src)

def _segment_sum(src, seg, n):
    return jax.ops.segment_sum(src, seg, n)
kernel_name = 'mk_dlrm_tower_d1_rec_r8_a6df5d'

def setup_inputs(seed: int=0):
    np.random.seed(seed)
    _w = jnp.asarray

    def _rec_inputs():
        import jax
        import jax.numpy as jnp
        _tk = jax.random.key(seed)
        dense_ctx = jax.random.normal(jax.random.fold_in(_tk, 190), (1024, 16), jnp.float32)
        ids = jnp.stack([jax.random.randint(jax.random.fold_in(_tk, 200 + f), (1024,), 0, v, jnp.int32) for f, v in enumerate([1000, 12500, 12500, 1000, 1000, 1000, 1250, 1250])], axis=1)
        tbl_0 = 0.05 * jax.random.normal(jax.random.fold_in(_tk, 500 + 0), (1000, 1024), jnp.float32)
        tbl_1 = 0.05 * jax.random.normal(jax.random.fold_in(_tk, 500 + 1), (12500, 1024), jnp.float32)
        tbl_2 = 0.05 * jax.random.normal(jax.random.fold_in(_tk, 500 + 2), (12500, 1024), jnp.float32)
        tbl_3 = 0.05 * jax.random.normal(jax.random.fold_in(_tk, 500 + 3), (1000, 1024), jnp.float32)
        tbl_4 = 0.05 * jax.random.normal(jax.random.fold_in(_tk, 500 + 4), (1000, 1024), jnp.float32)
        tbl_5 = 0.05 * jax.random.normal(jax.random.fold_in(_tk, 500 + 5), (1000, 1024), jnp.float32)
        tbl_6 = 0.05 * jax.random.normal(jax.random.fold_in(_tk, 500 + 6), (1250, 1024), jnp.float32)
        tbl_7 = 0.05 * jax.random.normal(jax.random.fold_in(_tk, 500 + 7), (1250, 1024), jnp.float32)
        _rk = jax.random.fold_in(_tk, 7)
        W_top1 = 0.0310087 * jax.random.normal(jax.random.fold_in(_tk, 801), (1040, 512), jnp.float32)
        W_top2 = 0.0441942 * jax.random.normal(jax.random.fold_in(_tk, 802), (512, 256), jnp.float32)
        W_top3 = 0.0625 * jax.random.normal(jax.random.fold_in(_tk, 803), (256, 1), jnp.float32)
        b_top1 = jnp.zeros((512,), jnp.float32)
        b_top2 = jnp.zeros((256,), jnp.float32)
        return (dense_ctx, ids, tbl_0, tbl_1, tbl_2, tbl_3, tbl_4, tbl_5, tbl_6, tbl_7, W_top1, b_top1, W_top2, b_top2, W_top3)
    dense_ctx, ids, tbl_0, tbl_1, tbl_2, tbl_3, tbl_4, tbl_5, tbl_6, tbl_7, W_top1, b_top1, W_top2, b_top2, W_top3 = _rec_inputs()

    def _L0_rec_setup():
        import jax, jax.numpy as jnp
        import numpy as np
        B, F, H = (1024, 8, 1024)

        def _linear_params(key, fan_in, fan_out):
            kw, kb = jax.random.split(key)
            w = jax.random.normal(kw, (fan_in, fan_out), dtype=jnp.float32) * 0.02
            b = jax.random.normal(kb, (fan_out,), dtype=jnp.float32) * 0.02
            return (w, b)
        key = jax.random.key(seed)
        ks = jax.random.split(key, 7)
        field_vectors = jax.random.normal(ks[0], (B, F, H), dtype=jnp.float32)
        Wn1, bn1 = _linear_params(ks[1], H, H)
        Wn2, bn2 = _linear_params(ks[2], H, H)
        Wa1, ba1 = _linear_params(ks[3], 2 * H, H)
        Wa2, ba2 = _linear_params(ks[4], H, H)
        Wo1, bo1 = _linear_params(ks[5], 2 * H, H)
        Wo2, bo2 = _linear_params(ks[6], H, H)
        not_idx = jnp.array([2, 3], dtype=jnp.int64)
        and_pairs = jnp.array([[0, 1], [2, 3]], dtype=jnp.int64)
        or_pairs = jnp.array([[4, 5]], dtype=jnp.int64)
        return {'field_vectors': field_vectors, 'Wn1': Wn1, 'bn1': bn1, 'Wn2': Wn2, 'bn2': bn2, 'Wa1': Wa1, 'ba1': ba1, 'Wa2': Wa2, 'ba2': ba2, 'Wo1': Wo1, 'bo1': bo1, 'Wo2': Wo2, 'bo2': bo2, 'not_idx': not_idx, 'and_pairs': and_pairs, 'or_pairs': or_pairs}
    _L0_rec_all = _L0_rec_setup()
    _L0_rec_in = {k: v for k, v in _L0_rec_all.items() if k in ('Wn1', 'bn1', 'Wn2', 'bn2', 'Wa1', 'ba1', 'Wa2', 'ba2', 'Wo1', 'bo1', 'Wo2', 'bo2', 'not_idx', 'and_pairs', 'or_pairs')}
    del _L0_rec_all
    return {'dense_ctx': dense_ctx, 'ids': ids, 'tbl_0': tbl_0, 'tbl_1': tbl_1, 'tbl_2': tbl_2, 'tbl_3': tbl_3, 'tbl_4': tbl_4, 'tbl_5': tbl_5, 'tbl_6': tbl_6, 'tbl_7': tbl_7, 'W_top1': W_top1, 'b_top1': b_top1, 'W_top2': W_top2, 'b_top2': b_top2, 'W_top3': W_top3, 'L0_rec_Wn1': _L0_rec_in['Wn1'], 'L0_rec_bn1': _L0_rec_in['bn1'], 'L0_rec_Wn2': _L0_rec_in['Wn2'], 'L0_rec_bn2': _L0_rec_in['bn2'], 'L0_rec_Wa1': _L0_rec_in['Wa1'], 'L0_rec_ba1': _L0_rec_in['ba1'], 'L0_rec_Wa2': _L0_rec_in['Wa2'], 'L0_rec_ba2': _L0_rec_in['ba2'], 'L0_rec_Wo1': _L0_rec_in['Wo1'], 'L0_rec_bo1': _L0_rec_in['bo1'], 'L0_rec_Wo2': _L0_rec_in['Wo2'], 'L0_rec_bo2': _L0_rec_in['bo2'], 'L0_rec_not_idx': _L0_rec_in['not_idx'], 'L0_rec_and_pairs': _L0_rec_in['and_pairs'], 'L0_rec_or_pairs': _L0_rec_in['or_pairs']}

def reference(dense_ctx, ids, tbl_0, tbl_1, tbl_2, tbl_3, tbl_4, tbl_5, tbl_6, tbl_7, W_top1, b_top1, W_top2, b_top2, W_top3, L0_rec_Wn1, L0_rec_bn1, L0_rec_Wn2, L0_rec_bn2, L0_rec_Wa1, L0_rec_ba1, L0_rec_Wa2, L0_rec_ba2, L0_rec_Wo1, L0_rec_bo1, L0_rec_Wo2, L0_rec_bo2, L0_rec_not_idx, L0_rec_and_pairs, L0_rec_or_pairs):
    import jax
    import jax.numpy as jnp

    def _L0_rec_ref(field_vectors, Wn1, bn1, Wn2, bn2, Wa1, ba1, Wa2, ba2, Wo1, bo1, Wo2, bo2, not_idx, and_pairs, or_pairs):
        import jax, jax.numpy as jnp
        import numpy as np
        B, F, H = (1024, 8, 1024)

        def _linear_params(key, fan_in, fan_out):
            kw, kb = jax.random.split(key)
            w = jax.random.normal(kw, (fan_in, fan_out), dtype=jnp.float32) * 0.02
            b = jax.random.normal(kb, (fan_out,), dtype=jnp.float32) * 0.02
            return (w, b)
        num_fields = field_vectors.shape[1]
        x_not = jnp.take(field_vectors, not_idx, axis=1)
        t = jnp.tanh(jax.nn.relu(x_not @ Wn1 + bn1) @ Wn2 + bn2)
        iv = field_vectors.at[:, not_idx, :].set(t)

        def pair_fuse(pairs, W1, b1, W2, b2):
            v = jnp.concatenate([jnp.take(iv, pairs[:, 0], axis=1), jnp.take(iv, pairs[:, 1], axis=1)], axis=-1)
            return jax.nn.relu(v @ W1 + b1) @ W2 + b2
        and_out = pair_fuse(and_pairs, Wa1, ba1, Wa2, ba2)
        or_out = pair_fuse(or_pairs, Wo1, bo1, Wo2, bo2)
        processed = jnp.zeros((num_fields,), dtype=field_vectors.dtype).at[and_pairs.reshape(-1)].set(1.0).at[or_pairs.reshape(-1)].set(1.0)
        remaining = 1.0 - processed
        sum_res = and_out.sum(axis=1) + or_out.sum(axis=1) + jnp.einsum('bfh,f->bh', iv, remaining)
        count = and_pairs.shape[0] + or_pairs.shape[0] + remaining.sum()
        return sum_res / count
    e = jnp.stack([tbl_0[ids[:, 0]], tbl_1[ids[:, 1]], tbl_2[ids[:, 2]], tbl_3[ids[:, 3]], tbl_4[ids[:, 4]], tbl_5[ids[:, 5]], tbl_6[ids[:, 6]], tbl_7[ids[:, 7]]], axis=1)
    z = _L0_rec_ref(e, L0_rec_Wn1, L0_rec_bn1, L0_rec_Wn2, L0_rec_bn2, L0_rec_Wa1, L0_rec_ba1, L0_rec_Wa2, L0_rec_ba2, L0_rec_Wo1, L0_rec_bo1, L0_rec_Wo2, L0_rec_bo2, L0_rec_not_idx, L0_rec_and_pairs, L0_rec_or_pairs)
    z = z.reshape(z.shape[0], -1)
    h = jnp.concatenate([z, dense_ctx], axis=1)
    h = jnp.maximum(h @ W_top1 + b_top1, 0.0)
    h = jnp.maximum(h @ W_top2 + b_top2, 0.0)
    y = h @ W_top3
    return y

_drawn_inputs = setup_inputs


def setup_inputs(seed=0):
    import zlib

    import numpy as np

    out = dict(_drawn_inputs(seed))
    spreads = {'b_top1': (0.0, 0.1), 'b_top2': (0.0, 0.1)}
    factors = {'tbl_0': 4.385,
     'tbl_1': 4.248,
     'tbl_2': 8.0,
     'tbl_3': 8.0,
     'tbl_4': 4.685,
     'tbl_5': 4.558,
     'L0_rec_Wn1': 8.0,
     'L0_rec_bn1': 8.0,
     'L0_rec_Wn2': 8.0,
     'L0_rec_bn2': 8.0,
     'L0_rec_Wa1': 2.819,
     'L0_rec_ba1': 3.897,
     'L0_rec_Wo1': 3.488,
     'L0_rec_bo1': 8.0,
     'L0_rec_Wo2': 2.939}
    for name, (base, spread) in spreads.items():
        noise = np.random.default_rng([zlib.crc32(name.encode()), seed]).standard_normal(out[name].shape)
        drawn = base * np.exp(spread * noise) if base else spread * noise
        out[name] = jnp.asarray(drawn.astype(out[name].dtype))
    for name, factor in factors.items():
        out[name] = (out[name] * factor).astype(out[name].dtype)
    return out
```

```python
import numpy as np
import concourse.bass as bass
from concourse import mybir
from contextlib import ExitStack

P = 128
B, F, H, DC = 1024, 8, 1024, 16
HALF = 512
NH = B // HALF
KC = H // P
TILES = HALF // P
VOCAB = [1000, 12500, 12500, 1000, 1000, 1000, 1250, 1250]
ROWS = sum(VOCAB)
T1, T2 = 512, 256
UCOL = KC * P
WRAW, WSPLIT = 4, 2
SKIP = 1 << 20

U_N1, U_N2, U_A1, U_O1, U_Z, U_T1, U_T2, UNITS = 0, 8, 16, 32, 48, 64, 68, 72
UT2 = 2 * P
B_N1, B_N2, B_A1, B_O1, B_A2, B_O2, B_T1, B_T2, B_COLS = 0, 8, 16, 24, 32, 40, 48, 52, 54
I_N, I_TAB, I_TSC, I_RTAB, I_RTSC, I_COLS = 0, 2, 8, 14, 22, 24


A_UNITS = 4 * KC


def units_before(h, phase):
    return A_UNITS + h * 72 + {1: 0, 2: 16, 3: 32, 4: 48, 5: 64, 6: 68, 7: 72}[phase]


def tiles_before(h, phase):
    return 4 * 16 + h * 38 + {1: 0, 2: 8, 3: 16, 4: 24, 5: 32, 6: 36, 7: 38}[phase]


def outs_before(h, phase):
    return 4 * 8 + h * 28 + {2: 0, 3: 8, 4: 16, 5: 24}[phase]


def fills_before(h, phase):
    return 48 + h * 56 + {1: 0, 2: 16, 3: 32, 4: 40}[phase]


def split_fills_before(h, phase):
    return fills_before(h, phase) - 8 * h - (8 if phase == 4 else 0)


def visits_before(h, phase):
    return 9 + h * 12 + {1: 0, 2: 4, 4: 8}[phase]


def tower(nc, tables, units, biases, bias_t, wt1d, wt3, dense_t, ids, fields, consts, ident_in, y_dram):
    f32, f32r, i32 = mybir.dt.float32, mybir.dt.float32r, mybir.dt.int32
    ALU, ACT, AX = mybir.AluOpType, mybir.ActivationFunctionType, mybir.AxisListType

    t_rows = [nc.dram_tensor(f"t_rows{h}", (2 * HALF, H), f32, kind="Internal").ap() for h in range(NH)]

    ctx = ExitStack()
    with ctx:
        def sb(name, shape, dt=f32):
            return ctx.enter_context(nc.sbuf_tensor(name, shape, dt))

        def sem(name):
            return ctx.enter_context(nc.semaphore(name))

        M = sb("M", [P, 4, KC, 2, HALF], f32r)
        acc = sb("acc", [P, KC, HALF])
        wraw = sb("wraw", [P, WRAW, UCOL])
        wsp = sb("wsp", [P, WSPLIT, 2, UCOL], f32r)
        rows = sb("rows", [P, 4, H])
        v = sb("v", [P, 2, HALF])
        stage = sb("stage", [P, 4, HALF])
        y_sb = v[0:1, 0, :]
        ident = sb("ident", [P, P])
        bias = sb("bias", [P, B_COLS])
        bias_z = sb("bias_z", [P, KC])
        w3 = sb("w3", [P, T2 // P])
        share = sb("share", [P, 1])
        lists = sb("lists", [P, I_COLS, 8], i32)

        taken = [0]

        def early(*dims):
            n = int(np.prod(dims))
            k, c = divmod(taken[0], HALF)
            assert c + n <= HALF or not c
            ap = acc[:, k, c:c + n]
            taken[0] += n
            return ap if len(dims) == 1 else ap.rearrange("p (a b) -> p a b", b=dims[1])

        ids_sb = early(8, F).bitcast(i32)
        cst = early(8 * F + 8 * F + 8)
        row_of = early(8, F)
        is_fld = early(8, F)
        prod = early(8, F)
        taken[0] = HALF
        lists_f = early(I_COLS, 8)
        fld_sb = early(8).bitcast(i32)
        fld = early(8)
        in0, in1, in_t = early(8), early(8), early(8)
        off = early(4, 8)
        processed = early(F)
        left = early(F)
        rk = early(2)
        count = early(1)

        gemm_ps = [ctx.enter_context(nc.psum_tensor(f"gemm_ps{i}", [P, HALF], f32)) for i in range(2)]
        fill_ps = [ctx.enter_context(nc.psum_tensor(f"fill_ps{i}", [P, HALF], f32)) for i in range(4)]
        t_ps = ctx.enter_context(nc.psum_tensor("t_ps", [P, TILES, P], f32))
        y_ps = ctx.enter_context(nc.psum_tensor("y_ps", [1, HALF], f32))

        lists_in = sem("lists_in")
        ident_in_sem = sem("ident_in_sem")
        small_in = sem("small_in")
        dense_in = sem("dense_in")
        raw_in = [sem(f"raw_in{s}") for s in range(WRAW)]
        w_hi = sem("w_hi")
        w_split = sem("w_split")
        unit_done = sem("unit_done")
        setup = sem("setup")
        lists_ready = sem("lists_ready")
        consts_ready = sem("consts_ready")
        row_tab = [sem(f"row_tab{s}") for s in range(4)]
        row_in = [sem(f"row_in{s}") for s in range(4)]
        rem_zero = sem("rem_zero")
        rem_in = [sem(f"rem_in{s}") for s in range(4)]
        fill_done = sem("fill_done")
        fill_hi = sem("fill_hi")
        fill_stored = sem("fill_stored")
        bank_read = sem("bank_read")
        out_done = sem("out_done")
        and_hi, and_split = sem("and_hi"), sem("and_split")
        z_hi, z_split = sem("z_hi"), sem("z_split")
        dense_hi, dense_split = sem("dense_hi"), sem("dense_split")
        n2_in = [sem(f"n2_in{s}") for s in range(2)]
        n2_hi, n2_split = sem("n2_hi"), sem("n2_split")
        rows_done = sem("rows_done")
        t_tanh = sem("t_tanh")
        t_stored = [sem(f"t_stored{s}") for s in range(2)]
        y_done, y_copied, y_out = sem("y_done"), sem("y_copied"), sem("y_out")

        def banks_read(n):
            return n + 2

        def outs(n):
            return n + 2

        def n2_raw(s):
            return acc[:, 4 + 2 * s:6 + 2 * s, :]

        A_MATS = [(0, 0), (0, 1), (1, 0), (1, 1)]
        B_SLOTS = {1: (2, 3), 2: (4, 5), 4: (0, 1)}

        block = ctx.enter_context(nc.Block())

        @block.sync
        def _(sp):
            def load_quad(first, q, cols=UCOL):
                for s in range(WRAW):
                    sp.wait_ge(w_split, 4 * q + s - WRAW + 1)
                    sp.dma_start(wraw[:, s, 0:cols], units[first + s, :, 0:cols]).then_inc(raw_in[s], 16)

            sp.dma_start(ids_sb, ids).then_inc(lists_in, 16)
            sp.dma_start(fld_sb, fields).then_inc(lists_in, 16)
            sp.dma_start(cst, consts).then_inc(lists_in, 16)
            sp.dma_start(ident[:, :], ident_in).then_inc(ident_in_sem, 16)
            for n in range(2):
                sp.dma_start(wraw[:, n, :], units[n, :, :]).then_inc(raw_in[n], 16)
            sp.dma_start(bias[:, :], biases).then_inc(small_in, 16)
            sp.dma_start(w3[:, :], wt3).then_inc(small_in, 16)
            sp.dma_start(stage[:, 0:2, :], bias_t).then_inc(small_in, 16)
            sp.wait_ge(row_in[TILES - 1], 16)
            for n in range(2, WRAW):
                sp.dma_start(wraw[:, n, :], units[n, :, :]).then_inc(raw_in[n], 16)

            def load_n2(k):
                sp.dma_start(n2_raw(k % 2), units[U_N2 + k, :, :].rearrange("p (f c) -> p f c", f=2)
                             ).then_inc(n2_in[k % 2], 16)

            for k in range(2):
                load_n2(k)
            load_quad(4, 1)
            for k in range(2, KC):
                sp.wait_ge(n2_split, k - 1)
                load_n2(k)
            with sp.Fori(1, 4) as g:
                with sp.Fori(0, 2) as i:
                    load_quad(4 * i, 2 * g + i)
            for h in range(NH):
                q = units_before(h, 1) // 4
                with sp.Fori(0, 4) as i:
                    load_quad(U_A1 + 4 * i, q + i)
                if h == 0:
                    for s in range(2):
                        sp.wait_ge(t_stored[s], 16 * 16)
                else:
                    sp.wait_ge(dense_split, h)
                sp.dma_start(stage[0:DC, 2, :], dense_t[:, h * HALF:(h + 1) * HALF]).then_inc(dense_in, 16)
                sp.dma_start(stage[0:DC, 3, :], wt1d).then_inc(dense_in, 16)
                with sp.Fori(0, 13) as i:
                    load_quad(U_A1 + 4 * i, q + 4 + i)
                load_quad(U_T2, q + 17, UT2)
            sp.wait_ge(y_out, 16 * NH)

        @block.gpsimd
        def _(pool):
            held = [0] * 4
            last_fill = [None] * 4

            def gather(dst, table, lst, tile, bound, where, op=ALU.bypass):
                pool.indirect_dma_start(
                    out=dst, out_offset=None, in_=table,
                    in_offset=bass.IndirectOffsetOnAxis(ap=lists[:, lst, tile:tile + 1], axis=0),
                    bounds_check=bound, oob_is_err=False, compute_op=op).then_inc(where, 16)

            def free_slot(x):
                if last_fill[x] is not None:
                    pool.wait_ge(fill_done, last_fill[x])

            def fetch_not(g, slots):
                half, slot = A_MATS[g]
                for t in range(TILES):
                    x = slots[t % len(slots)]
                    free_slot(x)
                    gather(rows[:, x, :], tables, I_N + slot, half * TILES + t, ROWS - 1, row_in[x])
                    last_fill[x] = 8 * g + 2 * t + 2

            def fetch(half, slot, first_fill, slots=(0, 1), between=None):
                for t in range(TILES):
                    x = slots[t % len(slots)]
                    free_slot(x)
                    gather(rows[:, x, :], tables, I_TAB + slot, half * TILES + t, ROWS - 1, row_tab[x])
                    if between is not None:
                        between(t)
                    held[x] += 1
                    pool.wait_ge(row_tab[x], 16 * held[x])
                    gather(rows[:, x, :], t_rows[half], I_TSC + slot, half * TILES + t, 2 * HALF - 1, row_in[x])
                    last_fill[x] = first_fill + 2 * t + 2

            def clear_remaining(h, tiles):
                for x, tile in tiles:
                    free_slot(x)
                    pool.memset(rows[:, x, :], 0.0).then_inc(rem_zero, 1)
                    last_fill[x] = fills_before(h, 3) + 2 * tile + 2

            def add_field(h, tiles, n):
                table, bound = (tables, ROWS - 1) if n < F else (t_rows[h], 2 * HALF - 1)
                for x, tile in tiles:
                    if n == 0:
                        pool.wait_ge(rem_zero, 4 * h + tile + 1)
                    else:
                        pool.wait_ge(rem_in[x], 16 * (10 * h + n))
                    gather(rows[:, x, :], table, I_RTAB + n, h * TILES + tile, bound, rem_in[x], ALU.add)

            pool.wait_ge(lists_ready, 1)
            fetch_not(0, (0, 1, 2, 3))
            pool.wait_ge(lists_ready, 2)
            for g in range(1, 4):
                fetch_not(g, (0, 1))
            pool.wait_ge(lists_ready, 3)
            for s in range(2):
                pool.wait_ge(t_stored[s], 16 * 4 * 3)
            for n in range(2):
                fetch(0, n, 32 + 8 * n, slots=(0, 1, 2, 3))
            for h in range(NH):
                early_tiles, late_tiles = ((2, 0), (3, 1)), ((0, 2), (1, 3))

                def add_early(first):
                    def step(t):
                        if first == -2 and t == 1:
                            clear_remaining(h, early_tiles)
                        if 0 <= first + t < F + 2:
                            add_field(h, early_tiles, first + t)
                    return step

                fetch(h, B_SLOTS[1][0], fills_before(h, 1), between=add_early(-2))
                fetch(h, B_SLOTS[1][1], fills_before(h, 1) + 8, between=add_early(2))
                fetch(h, B_SLOTS[2][0], fills_before(h, 2), between=add_early(6))
                fetch(h, B_SLOTS[2][1], fills_before(h, 2) + 8)
                clear_remaining(h, late_tiles)
                for n in range(F + 2):
                    add_field(h, late_tiles, n)
                if h == 0:
                    for s in range(2):
                        pool.wait_ge(t_stored[s], 16 * 4 * 4)
                if h + 1 < NH:
                    for n in range(2):
                        fetch(h + 1, B_SLOTS[4][n], fills_before(h, 4) + 8 * n)

        @block.tensor
        def _(pe):
            def w(s, hl, k):
                return wsp[:, s % WSPLIT, hl, k * P:(k + 1) * P]

            def three(ps, whi, wlo, xhi, xlo, first, last):
                pe.matmul(ps, whi, xhi, start=first, stop=False)
                pe.matmul(ps, whi, xlo, start=False, stop=False)
                return pe.matmul(ps, wlo, xhi, start=False, stop=last)

            def fill(n, s, slot):
                if not isinstance(n, int) or n >= 4:
                    pe.wait_ge(fill_stored, n - 3)
                for c in range(4):
                    k = 4 * (s % 2) + c
                    t = pe.transpose(fill_ps[s % 4][:, c * P:(c + 1) * P], rows[:, slot, k * P:(k + 1) * P],
                                     ident[:, :])
                t.then_inc(fill_done, 1)

            def quad(u, tile, parts, mats, fills=None, ready=None, tail=None, chunks=KC):
                for s in range(4):
                    m, part = s // parts, s % parts
                    ps = gemm_ps[m % 2][:, :]
                    if part == 0:
                        pe.wait_ge(bank_read, banks_read(tile + m - 1))
                    pe.wait_ge(w_split, u + s + 1)
                    for k in range(chunks):
                        if ready is not None and m == 0:
                            ready(part, k)
                        src = (part * chunks + k) if chunks < KC else k
                        first = part == 0 and k == 0
                        last = part == parts - 1 and k == chunks - 1 and tail is None
                        mm = three(ps, w(s, 0, k), w(s, 1, k), M[:, mats[part], src, 0, :],
                                   M[:, mats[part], src, 1, :], first, last)
                        if k == 5 and fills is not None:
                            fills(s)
                    if tail is not None:
                        mm = tail(ps, s)
                    mm.then_inc(unit_done, 1)

            def row_fills(n0, visit):
                def one(s):
                    if s % 2 == 0:
                        pe.wait_ge(row_in[s // 2], 16 * (visit + 1))
                    fill(n0 + s, s, s // 2)
                return one

            def slot_fills(n0, tile, visits):
                pe.wait_ge(row_in[tile], 16 * visits[tile // 2])
                for c in range(2):
                    fill(n0 + 2 * tile + c, 2 * tile + c, tile)

            pe.wait_ge(ident_in_sem, 16)
            for tile in range(TILES):
                slot_fills(0, tile, (1, 1))

            def stage_a(g, last):
                with pe.Fori(0, 2) as i:
                    def x_ready(part, k):
                        if k == 0:
                            pe.wait_ge(fill_stored, 8 * g + 8)

                    quad(8 * g + 4 * i, 16 * g + 4 * i, 1, [2], ready=x_ready)
                for f in range(2):
                    if last:
                        fills = (lambda j: slot_fills(32, j, (8, 2))) if f == 0 else None
                    else:
                        fills = row_fills(8 * g + 8 + 4 * f, 2 * g + 1 + f)
                    for j in range(TILES):
                        pe.wait_ge(bank_read, banks_read(16 * g + 8 + 4 * f + j - 1))
                        for k in range(KC):
                            if f == 0 and j == 0:
                                pe.wait_ge(n2_split, k + 1)
                                pe.wait_ge(out_done, outs(8 * g + k + 1))
                            col = slice(j * P, (j + 1) * P)
                            mm = three(gemm_ps[j % 2][:, :], M[:, 3, k, 0, col], M[:, 3, k, 1, col],
                                       M[:, f, k, 0, :], M[:, f, k, 1, :], k == 0, k == KC - 1)
                            if k == 5 and fills is not None:
                                fills(j)
                        mm.then_inc(rows_done, 1)

            with pe.Fori(0, 3) as g:
                stage_a(g, last=False)
            stage_a(3, last=True)
            for tile in range(TILES):
                slot_fills(40, tile, (9, 3))

            for h in range(NH):
                def and_like(phase, mats):
                    u, tile, n0 = units_before(h, phase), tiles_before(h, phase), fills_before(h, phase)

                    def filled(part, k):
                        if k == 0:
                            pe.wait_ge(fill_stored, n0 - 8 + 8 * part)

                    with pe.Fori(0, 4) as i:
                        quad(u + 4 * i, tile + 2 * i, 2, mats, ready=filled,
                             fills=row_fills(n0 + 4 * i, visits_before(h, phase) + i))

                and_like(1, [2, 3])
                and_like(2, [0, 1])
                u, tile = units_before(h, 3), tiles_before(h, 3)
                pe.wait_ge(fill_stored, fills_before(h, 3))
                with pe.Fori(0, 2) as i:
                    quad(u + 4 * i, tile + 2 * i, 2, [2, 3])
                for i in (2, 3):
                    def rem_fills(s):
                        slot = 2 + s // 2 if i == 2 else s // 2
                        if s % 2 == 0:
                            pe.wait_ge(rem_in[slot], 160 * (h + 1))
                        fill(fills_before(h, 3) + 4 * (i - 2) + s, s, slot)

                    quad(u + 4 * i, tile + 2 * i, 2, [2, 3], fills=rem_fills)

                u, tile = units_before(h, 4), tiles_before(h, 4)
                with pe.Fori(0, 4) as i:
                    def ready(part, k):
                        if part == 0:
                            pe.wait_ge(and_split, 8 * h + k + 1)
                        else:
                            pe.wait_ge(out_done, outs(outs_before(h, 3) + k + 1))

                    quad(u + 4 * i, tile + 2 * i, 2, [0, 1], ready=ready,
                         fills=row_fills(fills_before(h, 4) + 4 * i, visits_before(h, 4) + i) if h + 1 < NH else None)

                def z_ready(part, k):
                    pe.wait_ge(z_split, 8 * h + k + 1)

                def dense_tail(ps, s):
                    if s == 0:
                        pe.wait_ge(dense_split, h + 1)
                    col = slice(s * P, (s + 1) * P)
                    return three(ps, M[0:DC, 1, 5, 0, col], M[0:DC, 1, 5, 1, col],
                                 M[0:DC, 1, 4, 0, :], M[0:DC, 1, 4, 1, :], False, True)

                quad(units_before(h, 5), tiles_before(h, 5), 1, [0], ready=z_ready, tail=dense_tail)

                def top1_ready(part, k):
                    pe.wait_ge(out_done, outs(outs_before(h, 5) + 2 * part + k + 1))

                quad(units_before(h, 6), tiles_before(h, 6), 2, [1, 1], ready=top1_ready, chunks=2)
                pe.wait_ge(bank_read, banks_read(tiles_before(h, 7)))
                if h:
                    pe.wait_ge(y_copied, h)
                pe.wait_ge(small_in, 48)
                for c in range(2):
                    mm = pe.matmul(y_ps[:, :], w3[:, c:c + 1], stage[:, c, :], start=(c == 0), stop=(c == 1))
                mm.then_inc(y_done, 1)

        @block.scalar
        def _(act):
            def split_w(slot, u, q, cols=UCOL):
                act.wait_ge(raw_in[slot], 16 * (q + 1))
                act.activation(wsp[:, slot % WSPLIT, 0, 0:cols], wraw[:, slot, 0:cols], ACT.Copy).then_inc(w_hi, 1)

            def fill_in(n, s, mat, j):
                act.wait_ge(fill_done, n + 1)
                c0 = 4 * (s % 2)
                act.activation(M[:, mat, c0:c0 + 4, 0, bass.ds(j * P, P)],
                               fill_ps[s % 4][:, :].rearrange("p (c x) -> p c x", c=4), ACT.Copy).then_inc(fill_hi, 1)

            def quad(u, q, fills=None, out=None, cols=(UCOL, UCOL)):
                for s in range(4):
                    if fills is not None:
                        fills(s)
                    act.wait_ge(unit_done, u + s + 1)
                    if cols[s // 2]:
                        split_w((s + 2) % 4, u + s + 2, q + (s + 2) // 4, cols[s // 2])
                    if out is not None:
                        out(s)

            def v_slot(n):
                act.wait_ge(out_done, outs(n - 1))

            def relu_out(tile, n, m, x, b0, mat):
                ps = gemm_ps[x % 2][:, :]
                v_slot(n)
                act.activation(M[:, mat, m, 0, :], ps, ACT.Relu, bias=bias[:, bass.ds(b0 + m, 1)])
                act.activation(v[:, x % 2, :], ps, ACT.Relu, bias=bias[:, bass.ds(b0 + m, 1)]).then_inc(bank_read, 1)

            act.sem_inc(bank_read, 2)
            split_w(0, 0, 0)
            split_w(1, 1, 0)
            for n in range(8):
                fill_in(n, n, 2, n // 2)
            act.wait_ge(small_in, 48)

            for g in range(4):
                with act.Fori(0, 2) as i:
                    def hidden(s):
                        relu_out(16 * g + 4 * i + s, 8 * g + 4 * i + s, 4 * i + s, s, B_N1, 3)
                        if g == 0:
                            act.wait_ge(n2_in[s % 2], 32 * i + 16 * (s // 2 + 1))
                            act.activation(M[:, 0:2, 4 * i + s, 0, :], n2_raw(s % 2), ACT.Copy).then_inc(n2_hi, 1)

                    quad(8 * g + 4 * i, 2 * g + i, out=hidden)
                for f in range(2):
                    for j in range(TILES):
                        if g < 3:
                            fill_in(8 * g + 8 + 4 * f + j, j, 2, 2 * f + j // 2)
                        elif f == 0:
                            for c in range(2):
                                fill_in(32 + 2 * j + c, 2 * j + c, 2, j)
                        n = 8 * g + 4 * f + j
                        act.wait_ge(bank_read, banks_read(16 * g + 8 + 4 * f + j + 1))
                        act.activation(stage[:, 2 + j % 2, :], stage[:, 2 + j % 2, :], ACT.Tanh).then_inc(t_tanh, 1)
                        act.wait_ge(t_tanh, n + 1)
                        half, field = A_MATS[g]
                        r0 = field * HALF + j * P
                        act.dma_start(t_rows[half][r0:r0 + P, f * HALF:(f + 1) * HALF],
                                      stage[:, 2 + j % 2, :]).then_inc(t_stored[j % 2], 16)
            for n in range(8):
                fill_in(40 + n, n, 3, n // 2)

            for h in range(NH):
                u = units_before(h, 1)
                if h:
                    act.wait_ge(z_split, 8 * h)
                with act.Fori(0, 2) as a:
                    with act.Fori(0, 2) as b:
                        def out(s):
                            if s % 2:
                                m = 4 * a + 2 * b + s // 2
                                act.activation(acc[:, m, :], gemm_ps[s // 2][:, :], ACT.Relu,
                                               bias=bias[:, bass.ds(B_A1 + m, 1)]).then_inc(bank_read, 1)

                        def fills(s):
                            fill_in(fills_before(h, 1) + 8 * a + 4 * b + s, s, a, 2 * b + s // 2)

                        quad(u + 8 * a + 4 * b, u // 4 + 2 * a + b, fills, out)
                u = units_before(h, 2)
                if h:
                    act.wait_ge(y_out, 16 * h)
                with act.Fori(0, 2) as a:
                    with act.Fori(0, 2) as b:
                        def out(s):
                            if s % 2:
                                m = 4 * a + 2 * b + s // 2
                                v_slot(outs_before(h, 2) + m)
                                act.activation(v[:, s // 2, :], gemm_ps[s // 2][:, :], ACT.Relu,
                                               bias=bias[:, bass.ds(B_A1 + m, 1)]).then_inc(bank_read, 1)

                        def fills(s):
                            fill_in(fills_before(h, 2) + 8 * a + 4 * b + s, s, 2 + a, 2 * b + s // 2)

                        quad(u + 8 * a + 4 * b, u // 4 + 2 * a + b, fills, out)
                u = units_before(h, 3)
                for lo, hi in ((0, 2), (2, 4)):
                    with act.Fori(lo, hi) as i:
                        def out(s):
                            if s % 2:
                                m = 2 * i + s // 2
                                relu_out(tiles_before(h, 3) + m, outs_before(h, 3) + m, m, s // 2, B_O1, 1)
                            if lo == 0:
                                c = 4 * i + s
                                act.wait_ge(out_done, outs(outs_before(h, 2) + c + 1))
                                act.activation(M[:, 0, c, 0, :], acc[:, c, :], ACT.Copy).then_inc(and_hi, 1)

                        quad(u + 4 * i, u // 4 + i, out=out)
                u = units_before(h, 4)
                act.wait_ge(consts_ready, 1)

                def quad4(i, mat, j0):
                    def out(s):
                        if s % 2:
                            m = 2 * i + s // 2
                            v_slot(outs_before(h, 4) + m)
                            act.activation(v[:, s // 2, :], gemm_ps[s // 2][:, :], ACT.Identity,
                                           bias=bias_z[:, bass.ds(m, 1)], scale=share[:, 0:1]).then_inc(bank_read, 1)
                        if s == 2 and isinstance(i, int) and i == 3:
                            for m in range(KC - 1):
                                z_in(m)

                    def fills(s):
                        fill_in(fills_before(h, 4) + 4 * i + s, s, mat, j0 + s // 2)

                    quad(u + 4 * i, u // 4 + i, fills if h + 1 < NH else None, out)

                def z_in(m):
                    act.wait_ge(out_done, outs(outs_before(h, 4) + m + 1))
                    act.activation(M[:, 0, m, 0, :], acc[:, m, :], ACT.Copy).then_inc(z_hi, 1)

                with act.Fori(0, 2) as i:
                    quad4(i, 2, 2 * i)
                quad4(2, 3, 0)
                quad4(3, 3, 2)
                z_in(KC - 1)
                act.wait_ge(dense_in, 32 * (h + 1))
                act.activation(M[0:DC, 1, 4:6, 0, :], stage[0:DC, 2:4, :], ACT.Copy).then_inc(dense_hi, 1)
                u = units_before(h, 5)

                def out5(s):
                    relu_out(tiles_before(h, 5) + s, outs_before(h, 5) + s, s, s, B_T1, 1)

                quad(u, u // 4, out=out5, cols=(UCOL, UT2))
                u = units_before(h, 6)

                def out6(s):
                    if s % 2:
                        act.activation(stage[:, s // 2, :], gemm_ps[s // 2][:, :], ACT.Relu,
                                       bias=bias[:, B_T2 + s // 2:B_T2 + s // 2 + 1]).then_inc(bank_read, 1)

                quad(u, u // 4, out=out6, cols=(UT2, UCOL if h + 1 < NH else 0))
                act.wait_ge(out_done, outs(outs_before(h, 5) + 3))
                act.wait_ge(y_done, h + 1)
                act.activation(y_sb, y_ps[:, :], ACT.Copy).then_inc(y_copied, 1)
                act.wait_ge(y_copied, h + 1)
                act.dma_start(y_dram[h:h + 1, :], y_sb).then_inc(y_out, 16)

        @block.vector
        def _(dve):
            steps = [0]

            def chain(ins):
                steps[0] += 1
                ins.then_inc(setup, 1)
                dve.wait_ge(setup, steps[0])

            def tt(o, a, b, op):
                chain(dve.tensor_tensor(o, a, b, op))

            def ts(o, a, s1, s2, op0, op1=ALU.bypass):
                chain(dve.tensor_scalar(o, a, s1, s2, op0, op1))

            def over_tiles(x):
                return x.unsqueeze(1).to_broadcast([P, 8, 8])

            def per_row(x):
                return x.unsqueeze(2).to_broadcast([P, 8, 8])

            base = cst[:, 0:8 * F].rearrange("p (j f) -> p j f", f=F)
            f_no = cst[:, 8 * F:16 * F].rearrange("p (s f) -> p s f", f=F)
            sample = cst[:, 16 * F:16 * F + 8]
            dve.sem_inc(out_done, 2)
            dve.wait_ge(lists_in, 48)
            chain(dve.tensor_copy(row_of, ids_sb))
            chain(dve.tensor_copy(fld, fld_sb))
            tt(row_of, row_of, base, ALU.add)

            def table_rows(s):
                ts(is_fld[:, s, :], f_no[:, s, :], fld[:, s:s + 1], None, ALU.is_equal)
                tt(prod, row_of, over_tiles(is_fld[:, s, :]), ALU.mult)
                chain(dve.tensor_reduce(lists_f[:, I_N + s, :], prod, axis=AX.X, op=ALU.add))

            def split_w(slot, u, cols=UCOL):
                dve.wait_ge(w_hi, u + 1)
                dve.tensor_tensor(wsp[:, slot % WSPLIT, 1, 0:cols], wraw[:, slot, 0:cols],
                                  wsp[:, slot % WSPLIT, 0, 0:cols].bitcast(f32), ALU.subtract).then_inc(w_split, 1)

            def fill_in(n, s, mat, j):
                dve.wait_ge(fill_hi, n + 1)
                c0 = 4 * (s % 2)
                dve.tensor_tensor(M[:, mat, c0:c0 + 4, 1, bass.ds(j * P, P)],
                                  fill_ps[s % 4][:, :].rearrange("p (c x) -> p c x", c=4),
                                  M[:, mat, c0:c0 + 4, 0, bass.ds(j * P, P)].bitcast(f32),
                                  ALU.subtract).then_inc(fill_stored, 1)

            table_rows(0)
            dve.tensor_copy(lists[:, 0, :], lists_f[:, 0, :]).then_inc(lists_ready, 1)
            table_rows(1)
            dve.tensor_copy(lists[:, 1, :], lists_f[:, 1, :]).then_inc(lists_ready, 1)
            for s in range(2, 8):
                table_rows(s)
            split_w(0, 0)
            split_w(1, 1)
            for n in range(8):
                fill_in(n, n, 2, n // 2)

            def other_lists():
                ts(in0, fld, fld[:, 0:1], None, ALU.is_equal)
                ts(in1, fld, fld[:, 1:2], None, ALU.is_equal)
                tt(in_t, in0, in1, ALU.max)
                ts(off[:, 0, :], in_t, float(SKIP), None, ALU.mult)
                ts(off[:, 1, :], in_t, -float(SKIP), float(SKIP), ALU.mult, ALU.add)
                ts(off[:, 2, :], in0, -float(HALF), float(HALF), ALU.mult, ALU.add)
                tt(off[:, 1, :], off[:, 1, :], off[:, 2, :], ALU.add)
                for s in range(8):
                    dst = lists_f[:, I_N + s, :]
                    if s >= 2:
                        ts(dst, dst, off[:, 0, s:s + 1], None, ALU.add)
                        ts(lists_f[:, I_TSC + s - 2, :], sample, off[:, 1, s:s + 1], None, ALU.add)
                chain(dve.tensor_reduce(processed, is_fld[:, 2:8, :].rearrange("p s f -> p f s"),
                                        axis=AX.X, op=ALU.max))
                ts(left, processed, -1.0, 1.0, ALU.mult, ALU.add)
                chain(dve.tensor_reduce(count, left, axis=AX.X, op=ALU.add))
                ts(count, count, 3.0, None, ALU.add)
                chain(dve.reciprocal(share[:, :], count))
                tt(off[:, 2, :], is_fld[:, 0, :], is_fld[:, 1, :], ALU.max)
                ts(off[:, 2, :], off[:, 2, :], -1.0, 1.0, ALU.mult, ALU.add)
                tt(off[:, 2, :], off[:, 2, :], left, ALU.mult)
                ts(off[:, 2, :], off[:, 2, :], -float(SKIP), float(SKIP), ALU.mult, ALU.add)
                tt(lists_f[:, I_RTAB:I_RTAB + F, :], row_of.rearrange("p j f -> p f j"),
                   per_row(off[:, 2, :]), ALU.add)
                for k in range(2):
                    tt(off[:, 3, :], left, is_fld[:, k, :], ALU.mult)
                    chain(dve.tensor_reduce(rk[:, k:k + 1], off[:, 3, :], axis=AX.X, op=ALU.add))
                ts(off[:, 0, 0:1], in0[:, 1:2], -1.0, 1.0, ALU.mult, ALU.add)
                tt(rk[:, 1:2], rk[:, 1:2], off[:, 0, 0:1], ALU.mult)
                ts(rk, rk, -float(SKIP), float(SKIP), ALU.mult, ALU.add)
                for k in range(2):
                    ts(lists_f[:, I_RTSC + k, :], sample, rk[:, k:k + 1], float(k * HALF), ALU.add, ALU.add)
                dve.tensor_copy(lists[:, 2:, :], lists_f[:, 2:, :]).then_inc(lists_ready, 1)
                dve.wait_ge(small_in, 48)
                chain(dve.tensor_scalar(bias_z[:, :], bias[:, B_A2:B_A2 + KC], 2.0, None, ALU.mult))
                chain(dve.tensor_tensor(bias_z[:, :], bias_z[:, :], bias[:, B_O2:B_O2 + KC], ALU.add))
                dve.tensor_scalar(bias_z[:, :], bias_z[:, :], share[:, 0:1], None, ALU.mult).then_inc(consts_ready, 1)

            def quad(u, fills=None, out=None, cols=(UCOL, UCOL)):
                for s in range(4):
                    if fills is not None:
                        fills(s)
                    if cols[s // 2]:
                        split_w((s + 2) % 4, u + s + 2, cols[s // 2])
                    if out is not None:
                        out(s)

            def relu_lo(tile, m, x, mat):
                dve.wait_ge(bank_read, banks_read(tile + 1))
                dve.tensor_tensor(M[:, mat, m, 1, :], v[:, x % 2, :], M[:, mat, m, 0, :].bitcast(f32),
                                  ALU.subtract).then_inc(out_done, 1)

            def stage_a(g, first, last):
                with dve.Fori(0, 2) as i:
                    def hidden(s):
                        relu_lo(16 * g + 4 * i + s, 4 * i + s, s, 3)
                        if first:
                            k = 4 * i + s
                            dve.wait_ge(n2_hi, k + 1)
                            dve.tensor_tensor(M[:, 0:2, k, 1, :], n2_raw(s % 2), M[:, 0:2, k, 0, :].bitcast(f32),
                                              ALU.subtract).then_inc(n2_split, 1)

                    quad(8 * g + 4 * i, out=hidden)
                for f in range(2):
                    for j in range(TILES):
                        if not last:
                            fill_in(8 * g + 8 + 4 * f + j, j, 2, 2 * f + j // 2)
                        elif f == 0:
                            for c in range(2):
                                fill_in(32 + 2 * j + c, 2 * j + c, 2, j)
                        if not first or f or j >= 2:
                            dve.wait_ge(t_stored[j % 2], 16 * (4 * g + 2 * f + j // 2))
                        if first and not f and j == 0:
                            dve.wait_ge(small_in, 48)
                        dve.wait_ge(rows_done, 8 * g + 4 * f + j + 1)
                        dve.tensor_tensor(stage[:, 2 + j % 2, :], gemm_ps[j % 2][:, :], stage[:, f, :],
                                          ALU.add).then_inc(bank_read, 1)
                        if first and not f and j == 1:
                            other_lists()

            stage_a(0, first=True, last=False)
            with dve.Fori(1, 3) as g:
                stage_a(g, first=False, last=False)
            stage_a(3, first=False, last=True)
            for n in range(8):
                fill_in(40 + n, n, 3, n // 2)

            for h in range(NH):
                u = units_before(h, 1)
                with dve.Fori(0, 2) as a:
                    with dve.Fori(0, 2) as b:
                        quad(u + 8 * a + 4 * b, fills=lambda s: fill_in(
                            split_fills_before(h, 1) + 8 * a + 4 * b + s, s, a, 2 * b + s // 2))
                u = units_before(h, 2)
                with dve.Fori(0, 2) as a:
                    with dve.Fori(0, 2) as b:
                        def out(s):
                            if s % 2:
                                m = 4 * a + 2 * b + s // 2
                                dve.wait_ge(bank_read, banks_read(tiles_before(h, 2) + m + 1))
                                dve.tensor_tensor(acc[:, m, :], v[:, s // 2, :], acc[:, m, :],
                                                  ALU.add).then_inc(out_done, 1)

                        quad(u + 8 * a + 4 * b, out=out, fills=lambda s: fill_in(
                            split_fills_before(h, 2) + 8 * a + 4 * b + s, s, 2 + a, 2 * b + s // 2))
                u = units_before(h, 3)
                with dve.Fori(0, 2) as i:
                    def out(s):
                        if s % 2:
                            m = 2 * i + s // 2
                            relu_lo(tiles_before(h, 3) + m, m, s // 2, 1)
                        c = 4 * i + s
                        dve.wait_ge(and_hi, 8 * h + c + 1)
                        dve.tensor_tensor(M[:, 0, c, 1, :], acc[:, c, :], M[:, 0, c, 0, :].bitcast(f32),
                                          ALU.subtract).then_inc(and_split, 1)

                    quad(u + 4 * i, out=out)
                dve.wait_ge(and_split, 8 * (h + 1))
                for i in (2, 3):
                    def rem_in_acc(s):
                        n = fills_before(h, 3) + 4 * (i - 2) + s
                        dve.wait_ge(fill_done, n + 1)
                        j, c0 = 2 * (i - 2) + s // 2, 4 * (s % 2)
                        dve.tensor_copy(acc[:, c0:c0 + 4, j * P:(j + 1) * P],
                                        fill_ps[s % 4][:, :].rearrange("p (c x) -> p c x", c=4)
                                        ).then_inc(fill_stored, 1)

                    def out(s):
                        if s % 2:
                            m = 2 * i + s // 2
                            relu_lo(tiles_before(h, 3) + m, m, s // 2, 1)

                    quad(u + 4 * i, fills=rem_in_acc, out=out)
                u = units_before(h, 4)
                dve.wait_ge(fill_stored, fills_before(h, 4))

                def quad4(i, mat, j0):
                    def out(s):
                        if s % 2:
                            m = 2 * i + s // 2
                            dve.wait_ge(bank_read, banks_read(tiles_before(h, 4) + m + 1))
                            dve.scalar_tensor_tensor(acc[:, m, :], acc[:, m, :], share[:, 0:1],
                                                     v[:, s // 2, :], ALU.mult, ALU.add).then_inc(out_done, 1)
                        if s == 2 and isinstance(i, int) and i == 3:
                            for m in range(KC - 1):
                                z_in(m)

                    quad(u + 4 * i, out=out, fills=(lambda s: fill_in(
                        split_fills_before(h, 4) + 4 * i + s, s, mat, j0 + s // 2)) if h + 1 < NH else None)

                def z_in(m):
                    dve.wait_ge(z_hi, 8 * h + m + 1)
                    dve.tensor_tensor(M[:, 0, m, 1, :], acc[:, m, :], M[:, 0, m, 0, :].bitcast(f32),
                                      ALU.subtract).then_inc(z_split, 1)

                with dve.Fori(0, 2) as i:
                    quad4(i, 2, 2 * i)
                quad4(2, 3, 0)
                quad4(3, 3, 2)
                z_in(KC - 1)
                dve.wait_ge(dense_hi, h + 1)
                dve.tensor_tensor(M[0:DC, 1, 4:6, 1, :], stage[0:DC, 2:4, :], M[0:DC, 1, 4:6, 0, :].bitcast(f32),
                                  ALU.subtract).then_inc(dense_split, 1)
                u = units_before(h, 5)
                quad(u, out=lambda s: relu_lo(tiles_before(h, 5) + s, s, s, 1), cols=(UCOL, UT2))
                quad(units_before(h, 6), cols=(UT2, UCOL if h + 1 < NH else 0))


def kernel(**inputs):
    import concourse.bacc as bacc
    from concourse.bass_utils import run_bass_kernel_spmd

    a = {k: np.asarray(x) for k, x in inputs.items()}

    def cut(w):
        k, n = w.shape
        return w.reshape(k // H, KC, P, n // P, P).transpose(3, 0, 2, 1, 4).reshape(n // P, k // H, P, UCOL)

    n1, n2, a1, a2, o1, o2 = (a["L0_rec_W" + s] for s in ("n1", "n2", "a1", "a2", "o1", "o2"))
    t2 = a["W_top2"].reshape(2, 2, P, 2, P).transpose(3, 0, 2, 1, 4).reshape(4, P, UT2)
    t2 = np.concatenate([t2, t2, t2, t2], axis=2)
    units = np.concatenate([
        cut(n1).reshape(-1, P, UCOL), n2.reshape(KC, P, UCOL), cut(a1).reshape(-1, P, UCOL),
        cut(o1).reshape(-1, P, UCOL), np.concatenate([cut(a2), cut(o2)], axis=1).reshape(-1, P, UCOL),
        cut(a["W_top1"][:H]).reshape(-1, P, UCOL), t2])
    biases = np.concatenate([a[n].reshape(-1, P).T for n in (
        "L0_rec_bn1", "L0_rec_bn2", "L0_rec_ba1", "L0_rec_bo1", "L0_rec_ba2", "L0_rec_bo2", "b_top1", "b_top2")], axis=1)
    fields = np.concatenate([a["L0_rec_not_idx"].reshape(-1), a["L0_rec_and_pairs"].reshape(-1),
                             a["L0_rec_or_pairs"].reshape(-1)])
    first_row = np.cumsum([0] + VOCAB[:-1])
    consts = np.concatenate([
        np.tile(first_row, (P, 8)), np.tile(np.arange(F), (P, 8)),
        np.arange(P)[:, None] + P * (np.arange(8) % TILES)[None, :]], axis=1).astype(np.float32)
    arrays = {
        "tables": np.concatenate([a[f"tbl_{f}"] for f in range(F)]),
        "units": units, "biases": biases,
        "bias_t": np.broadcast_to(a["L0_rec_bn2"].reshape(1, 2, HALF), (P, 2, HALF)),
        "wt1d": a["W_top1"][H:], "wt3": a["W_top3"].reshape(2, P).T, "dense_t": a["dense_ctx"].T,
        "ids": a["ids"].reshape(8, P, F).transpose(1, 0, 2), "fields": np.tile(fields, (P, 1)),
        "consts": consts, "ident_in": np.eye(P, dtype=np.float32),
    }
    nc = bacc.Bacc("TRN2", target_bir_lowering=False, num_devices=1)
    feed, args = {}, []
    for name, x in arrays.items():
        x = np.ascontiguousarray(x)
        feed[name] = x
        args.append(nc.dram_tensor(name, x.shape, mybir.dt.from_np(x.dtype), kind="ExternalInput").ap())
    y = nc.dram_tensor("y", (NH, HALF), mybir.dt.float32, kind="ExternalOutput").ap()
    tower(nc, *args, y)
    r = run_bass_kernel_spmd(nc, [feed], core_ids=[0])
    return r.results[0]["y"].reshape(B, 1)
```

```python
import numpy as np
import concourse.bass as bass
from concourse import mybir
from contextlib import ExitStack

P = 128
B, F, H, DC = 1024, 8, 1024, 16
HALF = 512
NH = B // HALF
KC = H // P
TILES = HALF // P
VOCAB = [1000, 12500, 12500, 1000, 1000, 1000, 1250, 1250]
ROWS = sum(VOCAB)
T2 = 256
DSTACK = 2 * 32 + DC
UCOL = KC * P
WRAW, WSPLIT = 4, 2
FILL_AT = 5
SKIP = 1 << 20

U_N1, U_N2, U_A1, U_O1, U_Z, U_T1, U_T2, UNITS = 0, 8, 16, 32, 48, 64, 68, 72
UT2 = 2 * P
B_N1, B_N2, B_A1, B_O1, B_A2, B_O2, B_T1, B_T2, B_COLS = 0, 8, 16, 24, 32, 40, 48, 52, 54
I_N, I_TAB, I_TSC, I_RTAB, I_RTSC, I_COLS = 0, 2, 8, 14, 22, 24


A_UNITS = 4 * KC


def units_before(h, phase):
    return A_UNITS + h * 72 + {1: 0, 2: 16, 3: 32, 4: 48, 5: 64, 6: 68, 7: 72}[phase]


def tiles_before(h, phase):
    return 4 * 16 + h * 38 + {1: 0, 2: 8, 3: 16, 4: 24, 5: 32, 6: 36, 7: 38}[phase]


def outs_before(h, phase):
    return 4 * 8 + h * 28 + {2: 0, 3: 8, 4: 16, 5: 24}[phase]


def fills_before(h, phase):
    return 48 + h * 56 + {1: 0, 2: 16, 3: 32, 4: 40}[phase]


def split_fills_before(h, phase):
    return fills_before(h, phase) - 8 * h - (8 if phase == 4 else 0)


def visits_before(h, phase):
    return 9 + h * 12 + {1: 0, 2: 4, 4: 8}[phase]


def tower(nc, tables, units, biases, bias_t, wt3, dense, ids, fields, consts, ident_in, y_dram):
    f32, f32r, i32 = mybir.dt.float32, mybir.dt.float32r, mybir.dt.int32
    ALU, ACT, AX = mybir.AluOpType, mybir.ActivationFunctionType, mybir.AxisListType

    t_rows = [nc.dram_tensor(f"t_rows{h}", (2 * HALF, H), f32, kind="Internal").ap() for h in range(NH)]

    ctx = ExitStack()
    with ctx:
        def sb(name, shape, dt=f32):
            return ctx.enter_context(nc.sbuf_tensor(name, shape, dt))

        def sem(name):
            return ctx.enter_context(nc.semaphore(name))

        M = sb("M", [P, 4, KC, 2, HALF], f32r)
        acc = sb("acc", [P, KC, HALF])
        wraw = sb("wraw", [P, WRAW, UCOL])
        wsp = sb("wsp", [P, WSPLIT, 2, UCOL], f32r)
        rows = sb("rows", [P, 4, H])
        v = sb("v", [P, 2, HALF])
        stage = sb("stage", [P, 4, HALF])
        stacked = M[0:DSTACK, 1, 4, :, :]
        y_sb = stage[0:1, 0, :]
        ident = sb("ident", [P, P])
        bias = sb("bias", [P, B_COLS])
        bias_z = sb("bias_z", [P, KC])
        w3 = sb("w3", [P, T2 // P])
        share = sb("share", [P, 1])
        lists = sb("lists", [P, I_COLS, 8], i32)

        taken = [0]

        def early(*dims):
            n = int(np.prod(dims))
            k, c = divmod(taken[0], HALF)
            assert c + n <= HALF or not c
            ap = acc[:, k, c:c + n]
            taken[0] += n
            return ap if len(dims) == 1 else ap.rearrange("p (a b) -> p a b", b=dims[1])

        ids_sb = early(8, F).bitcast(i32)
        cst = early(8 * F + 8 * F + 8)
        row_of = early(8, F)
        is_fld = early(8, F)
        prod = early(8, F)
        taken[0] = HALF
        lists_f = early(I_COLS, 8)
        fld_sb = early(8).bitcast(i32)
        fld = early(8)
        in0, in1, in_t = early(8), early(8), early(8)
        off = early(4, 8)
        processed = early(F)
        left = early(F)
        rk = early(2)
        count = early(1)

        gemm_ps = [ctx.enter_context(nc.psum_tensor(f"gemm_ps{i}", [P, HALF], f32)) for i in range(2)]
        fill_ps = [ctx.enter_context(nc.psum_tensor(f"fill_ps{i}", [P, HALF], f32)) for i in range(4)]
        top2_ps = ctx.enter_context(nc.psum_tensor("top2_ps", [P, HALF], f32))
        y_ps = ctx.enter_context(nc.psum_tensor("y_ps", [1, HALF], f32))

        lists_in = sem("lists_in")
        ident_in_sem = sem("ident_in_sem")
        small_in = sem("small_in")
        dense_in = sem("dense_in")
        raw_in = [sem(f"raw_in{s}") for s in range(WRAW)]
        w_hi = sem("w_hi")
        w_split = sem("w_split")
        unit_done = sem("unit_done")
        setup = sem("setup")
        lists_ready = sem("lists_ready")
        consts_ready = sem("consts_ready")
        row_tab = [sem(f"row_tab{s}") for s in range(4)]
        row_in = [sem(f"row_in{s}") for s in range(4)]
        rem_zero = sem("rem_zero")
        rem_in = [sem(f"rem_in{s}") for s in range(4)]
        fill_done = sem("fill_done")
        fill_hi = sem("fill_hi")
        fill_stored = sem("fill_stored")
        bank_read = sem("bank_read")
        out_done = sem("out_done")
        and_hi, and_split = sem("and_hi"), sem("and_split")
        z_hi, z_split = sem("z_hi"), sem("z_split")
        dense_hi, dense_split = sem("dense_hi"), sem("dense_split")
        n2_in = [sem(f"n2_in{s}") for s in range(2)]
        n2_hi, n2_split = sem("n2_hi"), sem("n2_split")
        rows_done = sem("rows_done")
        t_tanh = sem("t_tanh")
        t_stored = [sem(f"t_stored{s}") for s in range(2)]
        y_done, y_copied, y_out = sem("y_done"), sem("y_copied"), sem("y_out")

        def banks_read(n):
            return n + 2

        def outs(n):
            return n + 2

        def n2_raw(s):
            return acc[:, 4 + 2 * s:6 + 2 * s, :]

        A_MATS = [(0, 0), (0, 1), (1, 0), (1, 1)]
        B_SLOTS = {1: (2, 3), 2: (4, 5), 4: (0, 1)}

        block = ctx.enter_context(nc.Block())

        @block.sync
        def _(sp):
            def load_quad(first, q, cols=UCOL):
                for s in range(WRAW):
                    sp.wait_ge(w_split, 4 * q + s - WRAW + 1)
                    sp.dma_start(wraw[:, s, 0:cols], units[first + s, :, 0:cols]).then_inc(raw_in[s], 16)

            sp.dma_start(ids_sb, ids).then_inc(lists_in, 16)
            sp.dma_start(fld_sb, fields).then_inc(lists_in, 16)
            sp.dma_start(cst, consts).then_inc(lists_in, 16)
            sp.dma_start(ident[:, :], ident_in).then_inc(ident_in_sem, 16)
            for n in range(2):
                sp.dma_start(wraw[:, n, :], units[n, :, :]).then_inc(raw_in[n], 16)
            sp.dma_start(bias[:, :], biases).then_inc(small_in, 16)
            sp.dma_start(w3[:, :], wt3).then_inc(small_in, 16)
            sp.dma_start(stage[:, 0:2, :], bias_t).then_inc(small_in, 16)
            sp.wait_ge(row_in[TILES - 1], 16)
            for n in range(2, WRAW):
                sp.dma_start(wraw[:, n, :], units[n, :, :]).then_inc(raw_in[n], 16)

            def load_n2(k):
                sp.dma_start(n2_raw(k % 2), units[U_N2 + k, :, :].rearrange("p (f c) -> p f c", f=2)
                             ).then_inc(n2_in[k % 2], 16)

            for k in range(2):
                load_n2(k)
            load_quad(4, 1)
            for k in range(2, KC):
                sp.wait_ge(n2_split, k - 1)
                load_n2(k)
            with sp.Fori(1, 4) as g:
                with sp.Fori(0, 2) as i:
                    load_quad(4 * i, 2 * g + i)
            for h in range(NH):
                q = units_before(h, 1) // 4
                with sp.Fori(0, 4) as i:
                    load_quad(U_A1 + 4 * i, q + i)
                if h == 0:
                    for s in range(2):
                        sp.wait_ge(t_stored[s], 16 * 16)
                else:
                    sp.wait_ge(dense_split, h)
                sp.dma_start(stage[0:DSTACK, 2:4, :], dense[h, :, :, :]).then_inc(dense_in, 16)
                with sp.Fori(0, 13) as i:
                    load_quad(U_A1 + 4 * i, q + 4 + i)
                load_quad(U_T2, q + 17, UT2)
            sp.wait_ge(y_out, 16 * NH)

        @block.gpsimd
        def _(pool):
            held = [0] * 4
            last_fill = [None] * 4

            def gather(dst, table, lst, tile, bound, where, op=ALU.bypass):
                pool.indirect_dma_start(
                    out=dst, out_offset=None, in_=table,
                    in_offset=bass.IndirectOffsetOnAxis(ap=lists[:, lst, tile:tile + 1], axis=0),
                    bounds_check=bound, oob_is_err=False, compute_op=op).then_inc(where, 16)

            def free_slot(x):
                if last_fill[x] is not None:
                    pool.wait_ge(fill_done, last_fill[x])

            def fetch_not(g, slots):
                half, slot = A_MATS[g]
                for t in range(TILES):
                    x = slots[t % len(slots)]
                    free_slot(x)
                    gather(rows[:, x, :], tables, I_N + slot, half * TILES + t, ROWS - 1, row_in[x])
                    last_fill[x] = 8 * g + 2 * t + 2

            def fetch(half, slot, first_fill, slots=(0, 1), between=None):
                for t in range(TILES):
                    x = slots[t % len(slots)]
                    free_slot(x)
                    gather(rows[:, x, :], tables, I_TAB + slot, half * TILES + t, ROWS - 1, row_tab[x])
                    if between is not None:
                        between(t)
                    held[x] += 1
                    pool.wait_ge(row_tab[x], 16 * held[x])
                    gather(rows[:, x, :], t_rows[half], I_TSC + slot, half * TILES + t, 2 * HALF - 1, row_in[x])
                    last_fill[x] = first_fill + 2 * t + 2

            def clear_remaining(h, tiles):
                for x, tile in tiles:
                    free_slot(x)
                    pool.memset(rows[:, x, :], 0.0).then_inc(rem_zero, 1)
                    last_fill[x] = fills_before(h, 3) + 2 * tile + 2

            def add_field(h, tiles, n):
                table, bound = (tables, ROWS - 1) if n < F else (t_rows[h], 2 * HALF - 1)
                for x, tile in tiles:
                    if n == 0:
                        pool.wait_ge(rem_zero, 4 * h + tile + 1)
                    else:
                        pool.wait_ge(rem_in[x], 16 * (10 * h + n))
                    gather(rows[:, x, :], table, I_RTAB + n, h * TILES + tile, bound, rem_in[x], ALU.add)

            pool.wait_ge(lists_ready, 1)
            fetch_not(0, (0, 1, 2, 3))
            pool.wait_ge(lists_ready, 2)
            for g in range(1, 4):
                fetch_not(g, (0, 1))
            pool.wait_ge(lists_ready, 3)
            for s in range(2):
                pool.wait_ge(t_stored[s], 16 * 4 * 3)
            for n in range(2):
                fetch(0, n, 32 + 8 * n, slots=(0, 1, 2, 3))
            for h in range(NH):
                early_tiles, late_tiles = ((2, 0), (3, 1)), ((0, 2), (1, 3))

                def add_early(first):
                    def step(t):
                        if first == -2 and t == 1:
                            clear_remaining(h, early_tiles)
                        if 0 <= first + t < F + 2:
                            add_field(h, early_tiles, first + t)
                    return step

                fetch(h, B_SLOTS[1][0], fills_before(h, 1), between=add_early(-2))
                fetch(h, B_SLOTS[1][1], fills_before(h, 1) + 8, between=add_early(2))
                fetch(h, B_SLOTS[2][0], fills_before(h, 2), between=add_early(6))
                fetch(h, B_SLOTS[2][1], fills_before(h, 2) + 8)
                clear_remaining(h, late_tiles)
                for n in range(F + 2):
                    add_field(h, late_tiles, n)
                if h == 0:
                    for s in range(2):
                        pool.wait_ge(t_stored[s], 16 * 4 * 4)
                if h + 1 < NH:
                    for n in range(2):
                        fetch(h + 1, B_SLOTS[4][n], fills_before(h, 4) + 8 * n)

        @block.tensor
        def _(pe):
            def w(s, hl, k):
                return wsp[:, s % WSPLIT, hl, k * P:(k + 1) * P]

            def three(ps, whi, wlo, xhi, xlo, first, last):
                pe.matmul(ps, whi, xhi, start=first, stop=False)
                pe.matmul(ps, whi, xlo, start=False, stop=False)
                return pe.matmul(ps, wlo, xhi, start=False, stop=last)

            def fill(n, s, slot):
                if not isinstance(n, int) or n >= 4:
                    pe.wait_ge(fill_stored, n - 3)
                for c in range(4):
                    k = 4 * (s % 2) + c
                    t = pe.transpose(fill_ps[s % 4][:, c * P:(c + 1) * P], rows[:, slot, k * P:(k + 1) * P],
                                     ident[:, :])
                t.then_inc(fill_done, 1)

            def quad(u, tile, parts, mats, fills=None, ready=None, tail=None):
                for s in range(4):
                    m, part = s // parts, s % parts
                    ps = gemm_ps[m % 2][:, :]
                    if part == 0:
                        pe.wait_ge(bank_read, banks_read(tile + m - 1))
                    pe.wait_ge(w_split, u + s + 1)
                    for k in range(KC):
                        if ready is not None and m == 0:
                            ready(part, k)
                        mm = three(ps, w(s, 0, k), w(s, 1, k), M[:, mats[part], k, 0, :], M[:, mats[part], k, 1, :],
                                   part == 0 and k == 0, part == parts - 1 and k == KC - 1 and tail is None)
                        if fills is not None:
                            fills(s, k)
                    if tail is not None:
                        mm = tail(ps, s)
                    mm.then_inc(unit_done, 1)

            def row_fills(n0, visit):
                def one(s, k):
                    if k == FILL_AT:
                        if s % 2 == 0:
                            pe.wait_ge(row_in[s // 2], 16 * (visit + 1))
                        fill(n0 + s, s, s // 2)
                return one

            def slot_fills(n0, tile, visits):
                pe.wait_ge(row_in[tile], 16 * visits[tile // 2])
                for c in range(2):
                    fill(n0 + 2 * tile + c, 2 * tile + c, tile)

            pe.wait_ge(ident_in_sem, 16)
            for tile in range(TILES):
                slot_fills(0, tile, (1, 1))

            def stage_a(g, last):
                with pe.Fori(0, 2) as i:
                    def x_ready(part, k):
                        if k == 0:
                            pe.wait_ge(fill_stored, 8 * g + 8)

                    quad(8 * g + 4 * i, 16 * g + 4 * i, 1, [2], ready=x_ready)
                for f in range(2):
                    if last:
                        fills = (lambda j, k: slot_fills(32, j, (8, 2)) if k == FILL_AT else None) if f == 0 else None
                    else:
                        fills = row_fills(8 * g + 8 + 4 * f, 2 * g + 1 + f)
                    for j in range(TILES):
                        pe.wait_ge(bank_read, banks_read(16 * g + 8 + 4 * f + j - 1))
                        for k in range(KC):
                            if f == 0 and j == 0:
                                pe.wait_ge(n2_split, k + 1)
                                pe.wait_ge(out_done, outs(8 * g + k + 1))
                            col = slice(j * P, (j + 1) * P)
                            mm = three(gemm_ps[j % 2][:, :], M[:, 3, k, 0, col], M[:, 3, k, 1, col],
                                       M[:, f, k, 0, :], M[:, f, k, 1, :], k == 0, k == KC - 1)
                            if fills is not None:
                                fills(j, k)
                        mm.then_inc(rows_done, 1)

            with pe.Fori(0, 3) as g:
                stage_a(g, last=False)
            stage_a(3, last=True)
            for h in range(NH):
                def and_like(phase, mats):
                    u, tile, n0 = units_before(h, phase), tiles_before(h, phase), fills_before(h, phase)

                    def filled(part, k):
                        if k == 0:
                            pe.wait_ge(fill_stored, n0 - 8 + 8 * part)

                    def first_fills(s, k):
                        if s == 0 and k < TILES:
                            slot_fills(40, k, (9, 3))
                        elif s == 1 and k == 2:
                            row_fills(n0, visits_before(h, phase))(0, FILL_AT)
                        elif s:
                            row_fills(n0, visits_before(h, phase))(s, k)

                    peeled = int(h == 0 and phase == 1)
                    if peeled:
                        quad(u, tile, 2, mats, ready=filled, fills=first_fills)
                    with pe.Fori(peeled, 4) as i:
                        quad(u + 4 * i, tile + 2 * i, 2, mats, ready=filled,
                             fills=row_fills(n0 + 4 * i, visits_before(h, phase) + i))

                and_like(1, [2, 3])
                and_like(2, [0, 1])
                u, tile = units_before(h, 3), tiles_before(h, 3)

                def or_filled(part, k):
                    if k == 0:
                        pe.wait_ge(fill_stored, fills_before(h, 3) - 8 + 8 * part)

                with pe.Fori(0, 2) as i:
                    quad(u + 4 * i, tile + 2 * i, 2, [2, 3], ready=or_filled)
                for i in (2, 3):
                    def rem_fills(s, k):
                        if k != FILL_AT:
                            return
                        slot = 2 + s // 2 if i == 2 else s // 2
                        if s % 2 == 0:
                            pe.wait_ge(rem_in[slot], 160 * (h + 1))
                        fill(fills_before(h, 3) + 4 * (i - 2) + s, s, slot)

                    quad(u + 4 * i, tile + 2 * i, 2, [2, 3], fills=rem_fills)

                u, tile = units_before(h, 4), tiles_before(h, 4)
                with pe.Fori(0, 4) as i:
                    def ready(part, k):
                        if part == 0:
                            pe.wait_ge(and_split, 8 * h + k + 1)
                        else:
                            pe.wait_ge(out_done, outs(outs_before(h, 3) + k + 1))

                    quad(u + 4 * i, tile + 2 * i, 2, [0, 1], ready=ready,
                         fills=row_fills(fills_before(h, 4) + 4 * i, visits_before(h, 4) + i) if h + 1 < NH else None)

                def z_ready(part, k):
                    pe.wait_ge(z_split, 8 * h + k + 1)

                def dense_tail(ps, s):
                    if s == 0:
                        pe.wait_ge(dense_split, h + 1)
                    return pe.matmul(ps, stacked[:, 1, s * P:(s + 1) * P], stacked[:, 0, :], start=False, stop=True)

                quad(units_before(h, 5), tiles_before(h, 5), 1, [0], ready=z_ready, tail=dense_tail)

                u, tile = units_before(h, 6), tiles_before(h, 6)
                banks = (gemm_ps[0], top2_ps)
                for s in range(4):
                    pair, m = divmod(s, 2)
                    if s < 2:
                        pe.wait_ge(bank_read, banks_read(tile - 1))
                    pe.wait_ge(w_split, u + s + 1)
                    for c in range(2):
                        k = 2 * pair + c
                        if m == 0:
                            pe.wait_ge(out_done, outs(outs_before(h, 5) + k + 1))
                        mm = three(banks[m][:, :], w(s, 0, c), w(s, 1, c), M[:, 1, k, 0, :], M[:, 1, k, 1, :],
                                   k == 0, k == 3)
                    mm.then_inc(unit_done, 1)
                if h:
                    pe.wait_ge(y_copied, h)
                pe.wait_ge(small_in, 48)
                for c in range(2):
                    pe.wait_ge(bank_read, banks_read(tile + c + 1))
                    mm = pe.matmul(y_ps[:, :], w3[:, c:c + 1], stage[:, c, :], start=(c == 0), stop=(c == 1))
                mm.then_inc(y_done, 1)

        @block.scalar
        def _(act):
            def split_w(slot, u, q, cols=UCOL):
                act.wait_ge(raw_in[slot], 16 * (q + 1))
                act.activation(wsp[:, slot % WSPLIT, 0, 0:cols], wraw[:, slot, 0:cols], ACT.Copy).then_inc(w_hi, 1)

            def fill_in(n, s, mat, j):
                act.wait_ge(fill_done, n + 1)
                c0 = 4 * (s % 2)
                act.activation(M[:, mat, c0:c0 + 4, 0, bass.ds(j * P, P)],
                               fill_ps[s % 4][:, :].rearrange("p (c x) -> p c x", c=4), ACT.Copy).then_inc(fill_hi, 1)

            def quad(u, q, fills=None, out=None, cols=(UCOL, UCOL), late=None):
                for s in range(4):
                    if fills is not None:
                        fills(s)
                    act.wait_ge(unit_done, u + s + 1)
                    short = cols[s // 2] == UT2
                    if short:
                        split_w((s + 2) % 4, u + s + 2, q + (s + 2) // 4, UT2)
                    if out is not None:
                        out(s)
                    if cols[s // 2] and not short:
                        split_w((s + 2) % 4, u + s + 2, q + (s + 2) // 4)
                    if late is not None:
                        late(s)

            def v_slot(n):
                act.wait_ge(out_done, outs(n - 1))

            def relu_out(tile, n, m, x, b0, mat):
                ps = gemm_ps[x % 2][:, :]
                v_slot(n)
                act.activation(M[:, mat, m, 0, :], ps, ACT.Relu, bias=bias[:, bass.ds(b0 + m, 1)])
                act.activation(v[:, x % 2, :], ps, ACT.Relu, bias=bias[:, bass.ds(b0 + m, 1)]).then_inc(bank_read, 1)

            act.sem_inc(bank_read, 2)
            split_w(0, 0, 0)
            split_w(1, 1, 0)
            for n in range(8):
                fill_in(n, n, 2, n // 2)
            act.wait_ge(small_in, 48)

            for g in range(4):
                with act.Fori(0, 2) as i:
                    def hidden(s):
                        relu_out(16 * g + 4 * i + s, 8 * g + 4 * i + s, 4 * i + s, s, B_N1, 3)

                    def n2_hi_part(s):
                        if g == 0:
                            act.wait_ge(n2_in[s % 2], 32 * i + 16 * (s // 2 + 1))
                            act.activation(M[:, 0:2, 4 * i + s, 0, :], n2_raw(s % 2), ACT.Copy).then_inc(n2_hi, 1)

                    quad(8 * g + 4 * i, 2 * g + i, out=hidden, late=n2_hi_part)
                for f in range(2):
                    for j in range(TILES):
                        if g < 3:
                            fill_in(8 * g + 8 + 4 * f + j, j, 2, 2 * f + j // 2)
                        elif f == 0:
                            for c in range(2):
                                fill_in(32 + 2 * j + c, 2 * j + c, 2, j)
                        n = 8 * g + 4 * f + j
                        act.wait_ge(bank_read, banks_read(16 * g + 8 + 4 * f + j + 1))
                        act.activation(stage[:, 2 + j % 2, :], stage[:, 2 + j % 2, :], ACT.Tanh).then_inc(t_tanh, 1)
                        act.wait_ge(t_tanh, n + 1)
                        half, field = A_MATS[g]
                        r0 = field * HALF + j * P
                        act.dma_start(t_rows[half][r0:r0 + P, f * HALF:(f + 1) * HALF],
                                      stage[:, 2 + j % 2, :]).then_inc(t_stored[j % 2], 16)
            for n in range(8):
                fill_in(40 + n, n, 3, n // 2)

            for h in range(NH):
                u = units_before(h, 1)
                if h:
                    act.wait_ge(z_split, 8 * h)
                with act.Fori(0, 2) as a:
                    with act.Fori(0, 2) as b:
                        def out(s):
                            if s % 2:
                                m = 4 * a + 2 * b + s // 2
                                act.activation(acc[:, m, :], gemm_ps[s // 2][:, :], ACT.Relu,
                                               bias=bias[:, bass.ds(B_A1 + m, 1)]).then_inc(bank_read, 1)

                        def fills(s):
                            fill_in(fills_before(h, 1) + 8 * a + 4 * b + s, s, a, 2 * b + s // 2)

                        quad(u + 8 * a + 4 * b, u // 4 + 2 * a + b, fills, out)
                u = units_before(h, 2)
                with act.Fori(0, 2) as a:
                    with act.Fori(0, 2) as b:
                        def out(s):
                            if s % 2:
                                m = 4 * a + 2 * b + s // 2
                                v_slot(outs_before(h, 2) + m)
                                act.activation(v[:, s // 2, :], gemm_ps[s // 2][:, :], ACT.Relu,
                                               bias=bias[:, bass.ds(B_A1 + m, 1)]).then_inc(bank_read, 1)

                        def fills(s):
                            fill_in(fills_before(h, 2) + 8 * a + 4 * b + s, s, 2 + a, 2 * b + s // 2)

                        quad(u + 8 * a + 4 * b, u // 4 + 2 * a + b, fills, out)
                u = units_before(h, 3)
                for lo, hi in ((0, 2), (2, 4)):
                    with act.Fori(lo, hi) as i:
                        def out(s):
                            if s % 2:
                                m = 2 * i + s // 2
                                relu_out(tiles_before(h, 3) + m, outs_before(h, 3) + m, m, s // 2, B_O1, 1)
                            if lo == 0:
                                c = 4 * i + s
                                act.wait_ge(out_done, outs(outs_before(h, 2) + c + 1))
                                act.activation(M[:, 0, c, 0, :], acc[:, c, :], ACT.Copy).then_inc(and_hi, 1)

                        quad(u + 4 * i, u // 4 + i, out=out)
                u = units_before(h, 4)
                act.wait_ge(consts_ready, 1)

                def quad4(i, mat, j0):
                    def out(s):
                        if s % 2:
                            m = 2 * i + s // 2
                            v_slot(outs_before(h, 4) + m)
                            act.activation(v[:, s // 2, :], gemm_ps[s // 2][:, :], ACT.Identity,
                                           bias=bias_z[:, bass.ds(m, 1)], scale=share[:, 0:1]).then_inc(bank_read, 1)

                    def late(s):
                        if s == 2 and isinstance(i, int) and i == 3:
                            for m in range(KC - 1):
                                z_in(m)

                    def fills(s):
                        fill_in(fills_before(h, 4) + 4 * i + s, s, mat, j0 + s // 2)

                    quad(u + 4 * i, u // 4 + i, fills if h + 1 < NH else None, out, late=late)

                def z_in(m):
                    act.wait_ge(out_done, outs(outs_before(h, 4) + m + 1))
                    act.activation(M[:, 0, m, 0, :], acc[:, m, :], ACT.Copy).then_inc(z_hi, 1)

                with act.Fori(0, 2) as i:
                    quad4(i, 2, 2 * i)
                quad4(2, 3, 0)
                quad4(3, 3, 2)
                z_in(KC - 1)
                act.wait_ge(dense_in, 16 * (h + 1))
                act.activation(stacked, stage[0:DSTACK, 2:4, :], ACT.Copy).then_inc(dense_hi, 1)
                u = units_before(h, 5)

                def out5(s):
                    relu_out(tiles_before(h, 5) + s, outs_before(h, 5) + s, s, s, B_T1, 1)

                quad(u, u // 4, out=out5, cols=(UCOL, UT2))
                u = units_before(h, 6)

                if h:
                    act.wait_ge(y_out, 16 * h)

                def out6(s):
                    if s >= 2:
                        act.activation(stage[:, s - 2, :], (gemm_ps[0], top2_ps)[s - 2][:, :], ACT.Relu,
                                       bias=bias[:, B_T2 + s - 2:B_T2 + s - 1]).then_inc(bank_read, 1)

                quad(u, u // 4, out=out6, cols=(UT2, UCOL if h + 1 < NH else 0))
                act.wait_ge(y_done, h + 1)
                act.activation(y_sb, y_ps[:, :], ACT.Copy).then_inc(y_copied, 1)
                act.wait_ge(y_copied, h + 1)
                act.dma_start(y_dram[h:h + 1, :], y_sb).then_inc(y_out, 16)

        @block.vector
        def _(dve):
            steps = [0]

            def chain(ins):
                steps[0] += 1
                ins.then_inc(setup, 1)
                dve.wait_ge(setup, steps[0])

            def tt(o, a, b, op):
                chain(dve.tensor_tensor(o, a, b, op))

            def ts(o, a, s1, s2, op0, op1=ALU.bypass):
                chain(dve.tensor_scalar(o, a, s1, s2, op0, op1))

            def over_tiles(x):
                return x.unsqueeze(1).to_broadcast([P, 8, 8])

            def per_row(x):
                return x.unsqueeze(2).to_broadcast([P, 8, 8])

            base = cst[:, 0:8 * F].rearrange("p (j f) -> p j f", f=F)
            f_no = cst[:, 8 * F:16 * F].rearrange("p (s f) -> p s f", f=F)
            sample = cst[:, 16 * F:16 * F + 8]
            dve.sem_inc(out_done, 2)
            dve.wait_ge(lists_in, 48)
            chain(dve.tensor_copy(row_of, ids_sb))
            chain(dve.tensor_copy(fld, fld_sb))
            tt(row_of, row_of, base, ALU.add)

            def table_rows(s):
                ts(is_fld[:, s, :], f_no[:, s, :], fld[:, s:s + 1], None, ALU.is_equal)
                tt(prod, row_of, over_tiles(is_fld[:, s, :]), ALU.mult)
                chain(dve.tensor_reduce(lists_f[:, I_N + s, :], prod, axis=AX.X, op=ALU.add))

            def split_w(slot, u, cols=UCOL):
                dve.wait_ge(w_hi, u + 1)
                dve.tensor_tensor(wsp[:, slot % WSPLIT, 1, 0:cols], wraw[:, slot, 0:cols],
                                  wsp[:, slot % WSPLIT, 0, 0:cols].bitcast(f32), ALU.subtract).then_inc(w_split, 1)

            def fill_in(n, s, mat, j):
                dve.wait_ge(fill_hi, n + 1)
                c0 = 4 * (s % 2)
                dve.tensor_tensor(M[:, mat, c0:c0 + 4, 1, bass.ds(j * P, P)],
                                  fill_ps[s % 4][:, :].rearrange("p (c x) -> p c x", c=4),
                                  M[:, mat, c0:c0 + 4, 0, bass.ds(j * P, P)].bitcast(f32),
                                  ALU.subtract).then_inc(fill_stored, 1)

            table_rows(0)
            dve.tensor_copy(lists[:, 0, :], lists_f[:, 0, :]).then_inc(lists_ready, 1)
            table_rows(1)
            dve.tensor_copy(lists[:, 1, :], lists_f[:, 1, :]).then_inc(lists_ready, 1)
            split_w(0, 0)
            split_w(1, 1)
            for n in range(8):
                fill_in(n, n, 2, n // 2)

            def pair_lists():
                ts(in0, fld, fld[:, 0:1], None, ALU.is_equal)
                ts(in1, fld, fld[:, 1:2], None, ALU.is_equal)
                tt(in_t, in0, in1, ALU.max)
                ts(off[:, 0, :], in_t, float(SKIP), None, ALU.mult)
                ts(off[:, 1, :], in_t, -float(SKIP), float(SKIP), ALU.mult, ALU.add)
                ts(off[:, 2, :], in0, -float(HALF), float(HALF), ALU.mult, ALU.add)
                tt(off[:, 1, :], off[:, 1, :], off[:, 2, :], ALU.add)
                for s in range(8):
                    dst = lists_f[:, I_N + s, :]
                    if s >= 2:
                        ts(dst, dst, off[:, 0, s:s + 1], None, ALU.add)
                        ts(lists_f[:, I_TSC + s - 2, :], sample, off[:, 1, s:s + 1], None, ALU.add)
                chain(dve.tensor_reduce(processed, is_fld[:, 2:8, :].rearrange("p s f -> p f s"),
                                        axis=AX.X, op=ALU.max))
                ts(left, processed, -1.0, 1.0, ALU.mult, ALU.add)
                chain(dve.tensor_reduce(count, left, axis=AX.X, op=ALU.add))
                ts(count, count, 3.0, None, ALU.add)
                chain(dve.reciprocal(share[:, :], count))

            def remaining_lists():
                tt(off[:, 2, :], is_fld[:, 0, :], is_fld[:, 1, :], ALU.max)
                ts(off[:, 2, :], off[:, 2, :], -1.0, 1.0, ALU.mult, ALU.add)
                tt(off[:, 2, :], off[:, 2, :], left, ALU.mult)
                ts(off[:, 2, :], off[:, 2, :], -float(SKIP), float(SKIP), ALU.mult, ALU.add)
                tt(lists_f[:, I_RTAB:I_RTAB + F, :], row_of.rearrange("p j f -> p f j"),
                   per_row(off[:, 2, :]), ALU.add)
                for k in range(2):
                    tt(off[:, 3, :], left, is_fld[:, k, :], ALU.mult)
                    chain(dve.tensor_reduce(rk[:, k:k + 1], off[:, 3, :], axis=AX.X, op=ALU.add))
                ts(off[:, 0, 0:1], in0[:, 1:2], -1.0, 1.0, ALU.mult, ALU.add)
                tt(rk[:, 1:2], rk[:, 1:2], off[:, 0, 0:1], ALU.mult)
                ts(rk, rk, -float(SKIP), float(SKIP), ALU.mult, ALU.add)
                for k in range(2):
                    ts(lists_f[:, I_RTSC + k, :], sample, rk[:, k:k + 1], float(k * HALF), ALU.add, ALU.add)
                dve.tensor_copy(lists[:, 2:, :], lists_f[:, 2:, :]).then_inc(lists_ready, 1)

            def z_bias():
                chain(dve.tensor_scalar(bias_z[:, :], bias[:, B_A2:B_A2 + KC], 2.0, None, ALU.mult))
                chain(dve.tensor_tensor(bias_z[:, :], bias_z[:, :], bias[:, B_O2:B_O2 + KC], ALU.add))
                dve.tensor_scalar(bias_z[:, :], bias_z[:, :], share[:, 0:1], None, ALU.mult).then_inc(consts_ready, 1)

            def quad(u, fills=None, out=None, cols=(UCOL, UCOL), late=None):
                for s in range(4):
                    if fills is not None:
                        fills(s)
                    short = cols[s // 2] == UT2
                    if short:
                        split_w((s + 2) % 4, u + s + 2, UT2)
                    if out is not None:
                        out(s)
                    if cols[s // 2] and not short:
                        split_w((s + 2) % 4, u + s + 2)
                    if late is not None:
                        late(s)

            def relu_lo(tile, m, x, mat):
                dve.wait_ge(bank_read, banks_read(tile + 1))
                dve.tensor_tensor(M[:, mat, m, 1, :], v[:, x % 2, :], M[:, mat, m, 0, :].bitcast(f32),
                                  ALU.subtract).then_inc(out_done, 1)

            def stage_a(g, first, last):
                with dve.Fori(0, 2) as i:
                    def hidden(s):
                        relu_lo(16 * g + 4 * i + s, 4 * i + s, s, 3)

                    def n2_lo_part(s):
                        if first:
                            k = 4 * i + s
                            dve.wait_ge(n2_hi, k + 1)
                            dve.tensor_tensor(M[:, 0:2, k, 1, :], n2_raw(s % 2), M[:, 0:2, k, 0, :].bitcast(f32),
                                              ALU.subtract).then_inc(n2_split, 1)

                    quad(8 * g + 4 * i, out=hidden, late=n2_lo_part)
                for f in range(2):
                    for j in range(TILES):
                        if not last:
                            fill_in(8 * g + 8 + 4 * f + j, j, 2, 2 * f + j // 2)
                        elif f == 0:
                            for c in range(2):
                                fill_in(32 + 2 * j + c, 2 * j + c, 2, j)
                        if not first or f or j >= 2:
                            dve.wait_ge(t_stored[j % 2], 16 * (4 * g + 2 * f + j // 2))
                        if first and not f and j == 0:
                            dve.wait_ge(small_in, 48)
                        dve.wait_ge(rows_done, 8 * g + 4 * f + j + 1)
                        dve.tensor_tensor(stage[:, 2 + j % 2, :], gemm_ps[j % 2][:, :], stage[:, f, :],
                                          ALU.add).then_inc(bank_read, 1)
                        if first and f == 0 and j < 3:
                            table_rows(2 + 2 * j)
                            table_rows(3 + 2 * j)
                        if first and (f, j) == (0, 3):
                            pair_lists()
                        if first and (f, j) == (1, 0):
                            remaining_lists()
                        if first and (f, j) == (1, 1):
                            z_bias()

            stage_a(0, first=True, last=False)
            with dve.Fori(1, 3) as g:
                stage_a(g, first=False, last=False)
            stage_a(3, first=False, last=True)
            for n in range(8):
                fill_in(40 + n, n, 3, n // 2)

            for h in range(NH):
                u = units_before(h, 1)
                with dve.Fori(0, 2) as a:
                    with dve.Fori(0, 2) as b:
                        quad(u + 8 * a + 4 * b, fills=lambda s: fill_in(
                            split_fills_before(h, 1) + 8 * a + 4 * b + s, s, a, 2 * b + s // 2))
                u = units_before(h, 2)
                with dve.Fori(0, 2) as a:
                    with dve.Fori(0, 2) as b:
                        def out(s):
                            if s % 2:
                                m = 4 * a + 2 * b + s // 2
                                dve.wait_ge(bank_read, banks_read(tiles_before(h, 2) + m + 1))
                                dve.tensor_tensor(acc[:, m, :], v[:, s // 2, :], acc[:, m, :],
                                                  ALU.add).then_inc(out_done, 1)

                        quad(u + 8 * a + 4 * b, out=out, fills=lambda s: fill_in(
                            split_fills_before(h, 2) + 8 * a + 4 * b + s, s, 2 + a, 2 * b + s // 2))
                u = units_before(h, 3)
                with dve.Fori(0, 2) as i:
                    def out(s):
                        if s % 2:
                            m = 2 * i + s // 2
                            relu_lo(tiles_before(h, 3) + m, m, s // 2, 1)
                        c = 4 * i + s
                        dve.wait_ge(and_hi, 8 * h + c + 1)
                        dve.tensor_tensor(M[:, 0, c, 1, :], acc[:, c, :], M[:, 0, c, 0, :].bitcast(f32),
                                          ALU.subtract).then_inc(and_split, 1)

                    quad(u + 4 * i, out=out)
                dve.wait_ge(and_split, 8 * (h + 1))
                for i in (2, 3):
                    def rem_in_acc(s):
                        n = fills_before(h, 3) + 4 * (i - 2) + s
                        dve.wait_ge(fill_done, n + 1)
                        j, c0 = 2 * (i - 2) + s // 2, 4 * (s % 2)
                        dve.tensor_copy(acc[:, c0:c0 + 4, j * P:(j + 1) * P],
                                        fill_ps[s % 4][:, :].rearrange("p (c x) -> p c x", c=4)
                                        ).then_inc(fill_stored, 1)

                    def out(s):
                        if s % 2:
                            m = 2 * i + s // 2
                            relu_lo(tiles_before(h, 3) + m, m, s // 2, 1)

                    quad(u + 4 * i, fills=rem_in_acc, out=out)
                u = units_before(h, 4)
                dve.wait_ge(fill_stored, fills_before(h, 4))

                def quad4(i, mat, j0):
                    def out(s):
                        if s % 2:
                            m = 2 * i + s // 2
                            dve.wait_ge(bank_read, banks_read(tiles_before(h, 4) + m + 1))
                            dve.scalar_tensor_tensor(acc[:, m, :], acc[:, m, :], share[:, 0:1],
                                                     v[:, s // 2, :], ALU.mult, ALU.add).then_inc(out_done, 1)

                    def late(s):
                        if s == 2 and isinstance(i, int) and i == 3:
                            for m in range(KC - 1):
                                z_in(m)

                    quad(u + 4 * i, out=out, late=late, fills=(lambda s: fill_in(
                        split_fills_before(h, 4) + 4 * i + s, s, mat, j0 + s // 2)) if h + 1 < NH else None)

                def z_in(m):
                    dve.wait_ge(z_hi, 8 * h + m + 1)
                    dve.tensor_tensor(M[:, 0, m, 1, :], acc[:, m, :], M[:, 0, m, 0, :].bitcast(f32),
                                      ALU.subtract).then_inc(z_split, 1)

                with dve.Fori(0, 2) as i:
                    quad4(i, 2, 2 * i)
                quad4(2, 3, 0)
                quad4(3, 3, 2)
                z_in(KC - 1)
                dve.wait_ge(dense_hi, h + 1)
                for side, p0 in ((0, 32), (1, 64)):
                    lo = stacked[p0:p0 + DC, side, :]
                    ins = dve.tensor_tensor(lo, stage[p0:p0 + DC, 2 + side, :], lo.bitcast(f32), ALU.subtract)
                ins.then_inc(dense_split, 1)
                u = units_before(h, 5)
                quad(u, out=lambda s: relu_lo(tiles_before(h, 5) + s, s, s, 1), cols=(UCOL, UT2))
                quad(units_before(h, 6), cols=(UT2, UCOL if h + 1 < NH else 0))


def kernel(**inputs):
    import concourse.bacc as bacc
    from concourse.bass_utils import run_bass_kernel_spmd

    a = {k: np.asarray(x) for k, x in inputs.items()}

    def cut(w):
        k, n = w.shape
        return w.reshape(k // H, KC, P, n // P, P).transpose(3, 0, 2, 1, 4).reshape(n // P, k // H, P, UCOL)

    n1, n2, a1, a2, o1, o2 = (a["L0_rec_W" + s] for s in ("n1", "n2", "a1", "a2", "o1", "o2"))
    t2 = a["W_top2"].reshape(2, 2, P, 2, P).transpose(0, 3, 2, 1, 4).reshape(4, P, UT2)
    t2 = np.concatenate([t2, t2, t2, t2], axis=2)
    units = np.concatenate([
        cut(n1).reshape(-1, P, UCOL), n2.reshape(KC, P, UCOL), cut(a1).reshape(-1, P, UCOL),
        cut(o1).reshape(-1, P, UCOL), np.concatenate([cut(a2), cut(o2)], axis=1).reshape(-1, P, UCOL),
        cut(a["W_top1"][:H]).reshape(-1, P, UCOL), t2])
    biases = np.concatenate([a[n].reshape(-1, P).T for n in (
        "L0_rec_bn1", "L0_rec_bn2", "L0_rec_ba1", "L0_rec_bo1", "L0_rec_ba2", "L0_rec_bo2", "b_top1", "b_top2")], axis=1)
    fields = np.concatenate([a["L0_rec_not_idx"].reshape(-1), a["L0_rec_and_pairs"].reshape(-1),
                             a["L0_rec_or_pairs"].reshape(-1)])
    first_row = np.cumsum([0] + VOCAB[:-1])
    consts = np.concatenate([
        np.tile(first_row, (P, 8)), np.tile(np.arange(F), (P, 8)),
        np.arange(P)[:, None] + P * (np.arange(8) % TILES)[None, :]], axis=1).astype(np.float32)
    dense = np.zeros((NH, DSTACK, 2, HALF), np.float32)
    for p0 in (0, 32, 64):
        dense[:, p0:p0 + DC, 0, :] = a["dense_ctx"].T.reshape(DC, NH, HALF).transpose(1, 0, 2)
        dense[:, p0:p0 + DC, 1, :] = a["W_top1"][H:]
    arrays = {
        "tables": np.concatenate([a[f"tbl_{f}"] for f in range(F)]),
        "units": units, "biases": biases,
        "bias_t": np.broadcast_to(a["L0_rec_bn2"].reshape(1, 2, HALF), (P, 2, HALF)),
        "wt3": a["W_top3"].reshape(2, P).T, "dense": dense,
        "ids": a["ids"].reshape(8, P, F).transpose(1, 0, 2), "fields": np.tile(fields, (P, 1)),
        "consts": consts, "ident_in": np.eye(P, dtype=np.float32),
    }
    nc = bacc.Bacc("TRN2", target_bir_lowering=False, num_devices=1)
    feed, args = {}, []
    for name, x in arrays.items():
        x = np.ascontiguousarray(x)
        feed[name] = x
        args.append(nc.dram_tensor(name, x.shape, mybir.dt.from_np(x.dtype), kind="ExternalInput").ap())
    y = nc.dram_tensor("y", (NH, HALF), mybir.dt.float32, kind="ExternalOutput").ap()
    tower(nc, *args, y)
    r = run_bass_kernel_spmd(nc, [feed], core_ids=[0])
    return r.results[0]["y"].reshape(B, 1)
```
